# Optimizing a Trainium2 kernel written in Bass

```python
import numpy as np
import jax
import jax.numpy as jnp

def _softmax(x, axis=-1):
    return jax.nn.softmax(x, axis=axis)

def _gelu(x):
    return jax.nn.gelu(x, approximate=True)

def _silu(x):
    return jax.nn.silu(x)

def _sigmoid(x):
    return jax.nn.sigmoid(x)

def _layernorm(x, axis=-1, eps=1e-05):
    m = jnp.mean(x, axis=axis, keepdims=True)
    v = jnp.var(x, axis=axis, keepdims=True)
    return (x - m) / jnp.sqrt(v + eps)

def _scatter_add(tgt, idx, src, axis=0):
    return tgt.at[idx].add(src)

def _segment_sum(src, seg, n):
    return jax.ops.segment_sum(src, seg, n)
kernel_name = 'mk_dlrm_tower_d1_rec_r8_fe985b'

def setup_inputs(seed: int=0):
    np.random.seed(seed)
    _w = jnp.asarray

    def _rec_inputs():
        import jax
        import jax.numpy as jnp
        _tk = jax.random.key(seed)
        dense_ctx = jax.random.normal(jax.random.fold_in(_tk, 190), (1024, 16), jnp.float32)
        ids = jnp.stack([jax.random.randint(jax.random.fold_in(_tk, 200 + f), (1024,), 0, v, jnp.int32) for f, v in enumerate([1250, 125000, 1250, 12500, 12500, 12500, 1000, 1250, 125000, 125000, 1250, 1000, 1250, 12500, 1000, 1250, 1250, 1000, 12500, 1000, 1000, 12500, 1250, 12500, 1000, 1250, 1250, 1000, 1250, 1250, 1250, 1250])], axis=1)
        tbl_0 = 0.05 * jax.random.normal(jax.random.fold_in(_tk, 500 + 0), (1250, 64), jnp.float32)
        tbl_1 = 0.05 * jax.random.normal(jax.random.fold_in(_tk, 500 + 1), (125000, 64), jnp.float32)
        tbl_2 = 0.05 * jax.random.normal(jax.random.fold_in(_tk, 500 + 2), (1250, 64), jnp.float32)
        tbl_3 = 0.05 * jax.random.normal(jax.random.fold_in(_tk, 500 + 3), (12500, 64), jnp.float32)
        tbl_4 = 0.05 * jax.random.normal(jax.random.fold_in(_tk, 500 + 4), (12500, 64), jnp.float32)
        tbl_5 = 0.05 * jax.random.normal(jax.random.fold_in(_tk, 500 + 5), (12500, 64), jnp.float32)
        tbl_6 = 0.05 * jax.random.normal(jax.random.fold_in(_tk, 500 + 6), (1000, 64), jnp.float32)
        tbl_7 = 0.05 * jax.random.normal(jax.random.fold_in(_tk, 500 + 7), (1250, 64), jnp.float32)
        tbl_8 = 0.05 * jax.random.normal(jax.random.fold_in(_tk, 500 + 8), (125000, 64), jnp.float32)
        tbl_9 = 0.05 * jax.random.normal(jax.random.fold_in(_tk, 500 + 9), (125000, 64), jnp.float32)
        tbl_10 = 0.05 * jax.random.normal(jax.random.fold_in(_tk, 500 + 10), (1250, 64), jnp.float32)
        tbl_11 = 0.05 * jax.random.normal(jax.random.fold_in(_tk, 500 + 11), (1000, 64), jnp.float32)
        tbl_12 = 0.05 * jax.random.normal(jax.random.fold_in(_tk, 500 + 12), (1250, 64), jnp.float32)
        tbl_13 = 0.05 * jax.random.normal(jax.random.fold_in(_tk, 500 + 13), (12500, 64), jnp.float32)
        tbl_14 = 0.05 * jax.random.normal(jax.random.fold_in(_tk, 500 + 14), (1000, 64), jnp.float32)
        tbl_15 = 0.05 * jax.random.normal(jax.random.fold_in(_tk, 500 + 15), (1250, 64), jnp.float32)
        tbl_16 = 0.05 * jax.random.normal(jax.random.fold_in(_tk, 500 + 16), (1250, 64), jnp.float32)
        tbl_17 = 0.05 * jax.random.normal(jax.random.fold_in(_tk, 500 + 17), (1000, 64), jnp.float32)
        tbl_18 = 0.05 * jax.random.normal(jax.random.fold_in(_tk, 500 + 18), (12500, 64), jnp.float32)
        tbl_19 = 0.05 * jax.random.normal(jax.random.fold_in(_tk, 500 + 19), (1000, 64), jnp.float32)
        tbl_20 = 0.05 * jax.random.normal(jax.random.fold_in(_tk, 500 + 20), (1000, 64), jnp.float32)
        tbl_21 = 0.05 * jax.random.normal(jax.random.fold_in(_tk, 500 + 21), (12500, 64), jnp.float32)
        tbl_22 = 0.05 * jax.random.normal(jax.random.fold_in(_tk, 500 + 22), (1250, 64), jnp.float32)
        tbl_23 = 0.05 * jax.random.normal(jax.random.fold_in(_tk, 500 + 23), (12500, 64), jnp.float32)
        tbl_24 = 0.05 * jax.random.normal(jax.random.fold_in(_tk, 500 + 24), (1000, 64), jnp.float32)
        tbl_25 = 0.05 * jax.random.normal(jax.random.fold_in(_tk, 500 + 25), (1250, 64), jnp.float32)
        tbl_26 = 0.05 * jax.random.normal(jax.random.fold_in(_tk, 500 + 26), (1250, 64), jnp.float32)
        tbl_27 = 0.05 * jax.random.normal(jax.random.fold_in(_tk, 500 + 27), (1000, 64), jnp.float32)
        tbl_28 = 0.05 * jax.random.normal(jax.random.fold_in(_tk, 500 + 28), (1250, 64), jnp.float32)
        tbl_29 = 0.05 * jax.random.normal(jax.random.fold_in(_tk, 500 + 29), (1250, 64), jnp.float32)
        tbl_30 = 0.05 * jax.random.normal(jax.random.fold_in(_tk, 500 + 30), (1250, 64), jnp.float32)
        tbl_31 = 0.05 * jax.random.normal(jax.random.fold_in(_tk, 500 + 31), (1250, 64), jnp.float32)
        _rk = jax.random.fold_in(_tk, 7)
        W_top1 = 0.0693375 * jax.random.normal(jax.random.fold_in(_tk, 801), (208, 512), jnp.float32)
        W_top2 = 0.0441942 * jax.random.normal(jax.random.fold_in(_tk, 802), (512, 256), jnp.float32)
        W_top3 = 0.0625 * jax.random.normal(jax.random.fold_in(_tk, 803), (256, 1), jnp.float32)
        b_top1 = jnp.zeros((512,), jnp.float32)
        b_top2 = jnp.zeros((256,), jnp.float32)
        return (dense_ctx, ids, tbl_0, tbl_1, tbl_2, tbl_3, tbl_4, tbl_5, tbl_6, tbl_7, tbl_8, tbl_9, tbl_10, tbl_11, tbl_12, tbl_13, tbl_14, tbl_15, tbl_16, tbl_17, tbl_18, tbl_19, tbl_20, tbl_21, tbl_22, tbl_23, tbl_24, tbl_25, tbl_26, tbl_27, tbl_28, tbl_29, tbl_30, tbl_31, W_top1, b_top1, W_top2, b_top2, W_top3)
    dense_ctx, ids, tbl_0, tbl_1, tbl_2, tbl_3, tbl_4, tbl_5, tbl_6, tbl_7, tbl_8, tbl_9, tbl_10, tbl_11, tbl_12, tbl_13, tbl_14, tbl_15, tbl_16, tbl_17, tbl_18, tbl_19, tbl_20, tbl_21, tbl_22, tbl_23, tbl_24, tbl_25, tbl_26, tbl_27, tbl_28, tbl_29, tbl_30, tbl_31, W_top1, b_top1, W_top2, b_top2, W_top3 = _rec_inputs()

    def _L0_rec_setup():
        import jax, jax.numpy as jnp
        import numpy as np
        B, F, D = (256, 32, 64)
        LAYER_SIZE = (128, 128)

        def _cin_layer(h, x0, W, b):
            bsz, H, d = h.shape
            M = x0.shape[1]
            z = jnp.einsum('bhd,bmd->bhmd', h, x0).reshape(bsz, H * M, d)
            out = jnp.einsum('bcd,oc->bod', z, W) + b[None, :, None]
            return jax.nn.relu(out)
        key = jax.random.key(seed)
        k1, k2, k3 = jax.random.split(key, 3)
        inputs = jax.random.normal(k1, (B, F, D), dtype=jnp.float32)
        W0 = jax.random.normal(k2, (LAYER_SIZE[0], F * F), dtype=jnp.float32) * 0.03
        b0 = jnp.zeros((LAYER_SIZE[0],), dtype=jnp.float32)
        W1 = jax.random.normal(k3, (LAYER_SIZE[1], LAYER_SIZE[0] // 2 * F), dtype=jnp.float32) * 0.03
        b1 = jnp.zeros((LAYER_SIZE[1],), dtype=jnp.float32)
        return {'inputs': inputs, 'W0': W0, 'b0': b0, 'W1': W1, 'b1': b1}
    _L0_rec_all = _L0_rec_setup()
    _L0_rec_in = {k: v for k, v in _L0_rec_all.items() if k in ('W0', 'b0', 'W1', 'b1')}
    del _L0_rec_all
    return {'dense_ctx': dense_ctx, 'ids': ids, 'tbl_0': tbl_0, 'tbl_1': tbl_1, 'tbl_2': tbl_2, 'tbl_3': tbl_3, 'tbl_4': tbl_4, 'tbl_5': tbl_5, 'tbl_6': tbl_6, 'tbl_7': tbl_7, 'tbl_8': tbl_8, 'tbl_9': tbl_9, 'tbl_10': tbl_10, 'tbl_11': tbl_11, 'tbl_12': tbl_12, 'tbl_13': tbl_13, 'tbl_14': tbl_14, 'tbl_15': tbl_15, 'tbl_16': tbl_16, 'tbl_17': tbl_17, 'tbl_18': tbl_18, 'tbl_19': tbl_19, 'tbl_20': tbl_20, 'tbl_21': tbl_21, 'tbl_22': tbl_22, 'tbl_23': tbl_23, 'tbl_24': tbl_24, 'tbl_25': tbl_25, 'tbl_26': tbl_26, 'tbl_27': tbl_27, 'tbl_28': tbl_28, 'tbl_29': tbl_29, 'tbl_30': tbl_30, 'tbl_31': tbl_31, 'W_top1': W_top1, 'b_top1': b_top1, 'W_top2': W_top2, 'b_top2': b_top2, 'W_top3': W_top3, 'L0_rec_W0': _L0_rec_in['W0'], 'L0_rec_b0': _L0_rec_in['b0'], 'L0_rec_W1': _L0_rec_in['W1'], 'L0_rec_b1': _L0_rec_in['b1']}

def reference(dense_ctx, ids, tbl_0, tbl_1, tbl_2, tbl_3, tbl_4, tbl_5, tbl_6, tbl_7, tbl_8, tbl_9, tbl_10, tbl_11, tbl_12, tbl_13, tbl_14, tbl_15, tbl_16, tbl_17, tbl_18, tbl_19, tbl_20, tbl_21, tbl_22, tbl_23, tbl_24, tbl_25, tbl_26, tbl_27, tbl_28, tbl_29, tbl_30, tbl_31, W_top1, b_top1, W_top2, b_top2, W_top3, L0_rec_W0, L0_rec_b0, L0_rec_W1, L0_rec_b1):
    import jax
    import jax.numpy as jnp

    def _L0_rec_ref(inputs, W0, b0, W1, b1):
        import jax, jax.numpy as jnp
        import numpy as np
        B, F, D = (256, 32, 64)
        LAYER_SIZE = (128, 128)

        def _cin_layer(h, x0, W, b):
            bsz, H, d = h.shape
            M = x0.shape[1]
            z = jnp.einsum('bhd,bmd->bhmd', h, x0).reshape(bsz, H * M, d)
            out = jnp.einsum('bcd,oc->bod', z, W) + b[None, :, None]
            return jax.nn.relu(out)
        out0 = _cin_layer(inputs, inputs, W0, b0)
        half = LAYER_SIZE[0] // 2
        next_hidden = out0[:, :half, :]
        direct0 = out0[:, half:, :]
        direct1 = _cin_layer(next_hidden, inputs, W1, b1)
        result = jnp.concatenate([direct0, direct1], axis=1)
        return jnp.sum(result, axis=-1)
    e = jnp.stack([tbl_0[ids[:, 0]], tbl_1[ids[:, 1]], tbl_2[ids[:, 2]], tbl_3[ids[:, 3]], tbl_4[ids[:, 4]], tbl_5[ids[:, 5]], tbl_6[ids[:, 6]], tbl_7[ids[:, 7]], tbl_8[ids[:, 8]], tbl_9[ids[:, 9]], tbl_10[ids[:, 10]], tbl_11[ids[:, 11]], tbl_12[ids[:, 12]], tbl_13[ids[:, 13]], tbl_14[ids[:, 14]], tbl_15[ids[:, 15]], tbl_16[ids[:, 16]], tbl_17[ids[:, 17]], tbl_18[ids[:, 18]], tbl_19[ids[:, 19]], tbl_20[ids[:, 20]], tbl_21[ids[:, 21]], tbl_22[ids[:, 22]], tbl_23[ids[:, 23]], tbl_24[ids[:, 24]], tbl_25[ids[:, 25]], tbl_26[ids[:, 26]], tbl_27[ids[:, 27]], tbl_28[ids[:, 28]], tbl_29[ids[:, 29]], tbl_30[ids[:, 30]], tbl_31[ids[:, 31]]], axis=1)
    z = _L0_rec_ref(e, L0_rec_W0, L0_rec_b0, L0_rec_W1, L0_rec_b1)
    z = z.reshape(z.shape[0], -1)
    h = jnp.concatenate([z, dense_ctx], axis=1)
    h = jnp.maximum(h @ W_top1 + b_top1, 0.0)
    h = jnp.maximum(h @ W_top2 + b_top2, 0.0)
    y = h @ W_top3
    return y

_drawn_inputs = setup_inputs


def setup_inputs(seed=0):
    import zlib

    import numpy as np

    out = dict(_drawn_inputs(seed))
    spreads = {'b_top1': (0.0, 2.0),
     'b_top2': (0.0, 0.8),
     'L0_rec_b0': (0.0, 0.1),
     'L0_rec_b1': (0.0, 0.593)}
    factors = {'tbl_0': 8.0,
     'tbl_1': 8.0,
     'tbl_2': 8.0,
     'tbl_3': 8.0,
     'tbl_4': 8.0,
     'tbl_5': 8.0,
     'tbl_6': 8.0,
     'tbl_7': 8.0,
     'tbl_8': 8.0,
     'tbl_9': 8.0,
     'tbl_10': 8.0,
     'tbl_11': 8.0,
     'tbl_12': 8.0,
     'tbl_13': 8.0,
     'tbl_14': 8.0,
     'tbl_15': 8.0,
     'tbl_16': 8.0,
     'tbl_17': 8.0,
     'tbl_18': 8.0,
     'tbl_19': 8.0,
     'tbl_20': 8.0,
     'tbl_21': 8.0,
     'tbl_22': 8.0,
     'tbl_23': 8.0,
     'tbl_24': 8.0,
     'tbl_25': 8.0,
     'tbl_26': 8.0,
     'tbl_27': 8.0,
     'tbl_28': 8.0,
     'tbl_29': 8.0,
     'tbl_30': 8.0,
     'tbl_31': 8.0,
     'L0_rec_W0': 8.0,
     'L0_rec_W1': 7.932,
     'dense_ctx': 8.0}
    for name, (base, spread) in spreads.items():
        noise = np.random.default_rng([zlib.crc32(name.encode()), seed]).standard_normal(out[name].shape)
        drawn = base * np.exp(spread * noise) if base else spread * noise
        out[name] = jnp.asarray(drawn.astype(out[name].dtype))
    for name, factor in factors.items():
        out[name] = (out[name] * factor).astype(out[name].dtype)
    return out
```

```python
from contextlib import ExitStack

import concourse.bass as bass
from concourse import mybir

F32 = mybir.dt.float32
F32R = mybir.dt.float32r
I32 = mybir.dt.int32
ALU = mybir.AluOpType
ACT = mybir.ActivationFunctionType
AX = mybir.AxisListType

P = 128
B = 1024
F = 32
D = 64
O = 128
H = O // 2
DENSE = 16
H1, H2 = 512, 256
BC = B // P
DPC = 4
C = DPC * P
GPB = D // DPC
T = BC * GPB
SHIFTS = F // 2

SLOTS = [("L1", 0), ("L0", 0), ("L0", 1), ("L1", 1), ("L1", 2),
         ("L1", 3), ("L1", 4), ("L1", 5), ("L1", 6), ("L1", 7)]
NS = len(SLOTS)
LAG = 4
LOW_LAG = 2
NZ = 5
PLAIN = 12
LATE = 5
WHO_FIRST = "VNVNVNVNVN"
WHO = "VGGGVGGGVG"


S_SQUARE = 1
S_STAGE = 3
S_TURN = 6
S_QUAD = 8
S_OUT1 = LAG - 1
S_L0_LAST = SLOTS.index(("L0", 1))
S_OUT0 = S_L0_LAST + LAG


def slots_of(t):
    if isinstance(t, int) and t < -1:
        return []
    if isinstance(t, int) and t < 0:
        return [s for s in range(NS) if SLOTS[s][0] == "L0"]
    if isinstance(t, int) and t == T - 1:
        return [s for s in range(NS) if SLOTS[s][0] == "L1"]
    return list(range(NS))


def who(t, s, first):
    return (WHO_FIRST if (t < PLAIN if isinstance(t, int) else first) else WHO)[s]


def count(which, t, s, first):
    if isinstance(t, int):
        return sum(who(u, v, None) in which for u in range(-1, t + 1) for v in slots_of(u) if u < t or v <= s)
    t0 = 0 if first else PLAIN
    each = sum(w in which for w in (WHO_FIRST if first else WHO))
    return t * each + (count(which, t0, s, None) - t0 * each)


def cin_tower(nc, dense, ids, tables, w0, b0, w1, b1, wt1, bt1, wt2, bt2, wt3, out):
    ctx = ExitStack()
    with ctx:
        def sb(name, shape, dt=F32):
            return ctx.enter_context(nc.sbuf_tensor(name, shape, dt))

        def ps(name, shape):
            return ctx.enter_context(nc.psum_tensor(name, shape, F32))

        def sem(name):
            return ctx.enter_context(nc.semaphore(name))

        emb = sb("emb", [P, BC * F, D])
        ids_sb = sb("ids_sb", [P, BC, F], I32)
        stage = sb("stage", [P, DPC, 2, 2, F], F32R)
        xhl0 = sb("xhl0", [P, C], F32R)
        xhl1 = sb("xhl1", [P, 2, C], F32R)
        x4 = sb("x4", [P, C])
        sq_r = sb("sq_r", [P, C], F32R)
        z = sb("z", [P, NZ, 2, C])
        z_hi = sb("z_hi", [P, NZ, 2, C], F32R)
        z_lo = sb("z_lo", [P, NZ, 2, C], F32R)
        hid2 = sb("hid2", [P, 2, C])
        direct = sb("direct", [P, C])
        rel1 = sb("rel1", [P, 2, C])
        acc0 = sb("acc0", [P, BC, C // 2])
        acc1 = sb("acc1", [P, BC, C // 2])
        ident = sb("ident", [P, P])
        ident_r = sb("ident_r", [P, P], F32R)
        sel_r = sb("sel_r", [P, F, H], F32R)
        rot_r = sb("rot_r", [P, SHIFTS, F], F32R)
        rep_r = sb("rep_r", [P, 4, F], F32R)
        w0_t = sb("w0_t", [P, SHIFTS // 4, O])
        w0_hi = sb("w0_hi", [P, SHIFTS // 4, O], F32R)
        w0_lo = sb("w0_lo", [P, SHIFTS // 4, O], F32R)
        w1_hi = sb("w1_hi", [P, F // 2, O], F32R)
        w1_lo = sb("w1_lo", [P, F // 2, O], F32R)
        w0_sq = sb("w0_sq", [P, O])
        w0_sq_r = sb("w0_sq_r", [P, O], F32R)
        w1_t = sb("w1_t", [P, F // 2, O])
        b0_sb = sb("b0_sb", [P, 1])
        b1_sb = sb("b1_sb", [P, 1])
        wt3_sb = sb("wt3_sb", [P, H2 // P])
        bt1_sb = sb("bt1_sb", [P, H1 // P])
        bt2_sb = sb("bt2_sb", [P, H2 // P])
        wt1a = sb("wt1a", [P, H1])
        scr = z[:, :, :, :].rearrange("p a b c -> p (a b c)")
        w0_sb, w0_sym = scr[:, 0:F * F], scr[:, F * F:2 * F * F]
        w0_pair = scr[:, 2 * F * F:2 * F * F + SHIFTS * F].rearrange("p (s i) -> p s i", i=F)
        w0_diag = scr[:, 3 * F * F:3 * F * F + P].rearrange("p (r i) -> p r i", i=F)
        fold = scr[:, 4 * F * F:4 * F * F + 2 * F]
        w1_sb = acc1[:, :, :].rearrange("p a b -> p (a b)")
        w1_mh = acc0[:, :, :].rearrange("p a b -> p (a b)")
        top = emb[:, :, :].rearrange("p a d -> p (a d)")
        feat_a, feat_b = top[:, 0:B], top[:, B:2 * B]
        h1_sb = top[:, 2 * B:2 * B + 4 * B].rearrange("p (k b) -> p k b", b=B)
        h2_sb = top[:, 6 * B:8 * B].rearrange("p (k b) -> p k b", b=B)
        y_sb = top[0:1, 8 * B:9 * B]
        off = LATE * F * D
        wt1b = top[:, off:off + H1]
        off += H1
        wt2_sb = top[:, off:off + H1 // P * H2].rearrange("p (k n) -> p k n", n=H2)
        off += H1 // P * H2
        dense_sb = top[:, off:off + BC * DENSE].rearrange("p (c f) -> p c f", f=DENSE)

        pair = [ps(f"pair{i}", [P, 2, C]) for i in range(2)]
        p_out1 = ps("p_out1", [P, 2, C])
        p_out0 = ps("p_out0", [P, C])
        p_x = ps("p_x", [P, C])

        ids_loaded = sem("ids_loaded")
        w_loaded = sem("w_loaded")
        top_loaded = sem("top_loaded")
        gathered = [sem(f"gathered{i}") for i in range(BC)]
        emb_ready = sem("emb_ready")
        pool_made = sem("pool_made")
        ident_ready = sem("ident_ready")
        consts_ready = sem("consts_ready")
        w0_added = sem("w0_added")
        w0_folded = sem("w0_folded")
        w_turned = sem("w_turned")
        w_copied = sem("w_copied")
        acc_cleared = sem("acc_cleared")
        hi_staged = sem("hi_staged")
        w_split = sem("w_split")
        sq_ready = sem("sq_ready")
        zh_ready = sem("zh_ready")
        zl_vector = sem("zl_vector")
        zl_pool = sem("zl_pool")
        staged = sem("staged")
        transposed = sem("transposed")
        xhl0_ready = sem("xhl0_ready")
        xhl1_ready = sem("xhl1_ready")
        squared = sem("squared")
        quad_ready = sem("quad_ready")
        x4_ready = sem("x4_ready")
        selected = sem("selected")
        z_ready = sem("z_ready")
        contracted = sem("contracted")
        out0_ready = sem("out0_ready")
        hid_ready = sem("hid_ready")
        direct_ready = sem("direct_ready")
        direct_used = sem("direct_used")
        rel1_ready = sem("rel1_ready")
        rel1_used = sem("rel1_used")
        dense_turned = sem("dense_turned")
        feat_cleared = sem("feat_cleared")
        feat_ready = sem("feat_ready")
        dense_ready = sem("dense_ready")
        top_mm = sem("top_mm")
        top_act = sem("top_act")
        stored = sem("stored")

        block = ctx.enter_context(nc.Block())

        def steps(eng, step):
            for t in (-2, -1, 0, 1):
                step(t)
            with eng.Fori(1, PLAIN // 2, 1) as i:
                step(2 * i, 0, True)
                step(2 * i + 1, 1, True)
            step(PLAIN)
            step(PLAIN + 1)
            with eng.Fori(PLAIN // 2 + 1, T // 2 - 1, 1) as i:
                step(2 * i, 0, False)
                step(2 * i + 1, 1, False)
            step(T - 2)
            step(T - 1)

        def has(t, k):
            return not isinstance(t, int) or 0 <= t + k < T

        BATCHES = [1, 4, 4, 4, 4, 4]
        TOP_ACTS = 2 * (H1 // P) + 2 * (H2 // P) + 2

        def turned(n):
            return pair[n % 2][:, 0, :]

        TOP_BANKS = [pair[0][:, 0, :], pair[0][:, 1, :], pair[1][:, 0, :], pair[1][:, 1, :]]

        def top_bank(n):
            return TOP_BANKS[n % 4]

        def pos(t, s):
            if isinstance(t, int):
                return count("NVG", t, s, None) - 1
            return t * NS + (pos(0, s))

        def at(t, p, s, n):
            return pos(t, s) % n if isinstance(t, int) else (p * NS + pos(0, s)) % n

        def lagged(t, p, first, n, lag):
            slots = slots_of(t)
            if n >= lag:
                return t, p, first, slots[n - lag]
            if isinstance(t, int) and t < 1:
                before = [(u, u % 2, None, s) for u in range(0, t) for s in slots_of(u)]
                k = len(before) - lag + n
                return before[k] if k >= 0 else None
            return t - 1, 1 - p, first, NS - lag + n

        def rest(t, lag):
            return [(t, t % 2, None, s) for s in slots_of(t)[-lag:]] if t in (-1, T - 1) else []

        W_LOADS = 4
        TOP_LOADS = 8

        @block.sync
        def _(sp):
            sp.dma_start(ids_sb[:, :, :], ids.rearrange("(c p) f -> p c f", p=P)).then_inc(ids_loaded, 16)
            sp.dma_start(w0_sb, w0).then_inc(w_loaded, 16)
            sp.dma_start(w1_sb, w1).then_inc(w_loaded, 16)
            sp.dma_start(b0_sb[:, :], b0.rearrange("(p a) -> p a", a=1)).then_inc(w_loaded, 16)
            sp.dma_start(b1_sb[:, :], b1.rearrange("(p a) -> p a", a=1)).then_inc(w_loaded, 16)
            sp.wait_ge(feat_cleared, 1)
            sp.dma_start(wt1a[0:DENSE, :], wt1[O + H:O + H + DENSE, :]).then_inc(top_loaded, 16)
            sp.dma_start(wt1a[H:P, :], wt1[0:H, :]).then_inc(top_loaded, 16)
            sp.dma_start(wt3_sb[:, :], wt3.rearrange("(k p) n -> p (k n)", p=P),
                         allow_slow_non_contiguous=True).then_inc(top_loaded, 16)
            sp.dma_start(bt1_sb[:, :], bt1.rearrange("(k p) -> p k", p=P),
                         allow_slow_non_contiguous=True).then_inc(top_loaded, 16)
            sp.dma_start(bt2_sb[:, :], bt2.rearrange("(k p) -> p k", p=P),
                         allow_slow_non_contiguous=True).then_inc(top_loaded, 16)
            sp.wait_ge(staged, (LATE + 1) * GPB)
            sp.dma_start(wt1b[:, :], wt1[H:H + O, :]).then_inc(top_loaded, 16)
            sp.dma_start(wt2_sb[:, :, :], wt2.rearrange("(k p) n -> p k n", p=P)).then_inc(top_loaded, 16)
            sp.dma_start(dense_sb[:, :, :], dense.rearrange("(c p) f -> p c f", p=P)).then_inc(top_loaded, 16)
            sp.wait_ge(top_act, TOP_ACTS)
            sp.dma_start(out.rearrange("b a -> a b"), y_sb).then_inc(stored, 16)
            sp.wait_ge(stored, 16)

        @block.gpsimd
        def _(pool):
            def gather(c, fields):
                for f in fields:
                    pool.indirect_dma_start(
                        emb[:, c * F + f, :], None, tables[f],
                        bass.IndirectOffsetOnAxis(ap=ids_sb[:, c, f:f + 1], axis=0),
                    ).then_inc(gathered[c], 16)

            EARLY = 3
            made = [0]

            def after(ins):
                made[0] += 1
                ins.then_inc(pool_made, 1)
                pool.wait_ge(pool_made, made[0])

            after(pool.memset(ident[:, :], 0.0))
            pool.affine_select(out=ident[:, :], in_=ident[:, :], compare_op=ALU.not_equal, fill=1.0, base=0,
                               pattern=[[-1, P]], channel_multiplier=1).then_inc(ident_ready, 1)
            after(pool.memset(fold[:, :], 0.0))
            for base in range(F, -P, -F):
                after(pool.affine_select(out=fold[:, :], in_=fold[:, :], compare_op=ALU.not_equal, fill=1.0,
                                         base=base, pattern=[[-1, 2 * F]], channel_multiplier=1))
            pool.tensor_copy(fold[:, 0:1], fold[:, 0:1]).then_inc(ident_ready, 1)
            pool.wait_ge(ids_loaded, 16)
            gather(0, range(F))
            for c in range(BC):
                if c + 1 < BC:
                    gather(c + 1, range(EARLY))
                pool.wait_ge(gathered[c], 16 * F)
                pool.sem_inc(emb_ready, 1)
                if c + 1 < BC:
                    gather(c + 1, range(EARLY, F))

            def low_part(t, p, first, s):
                if who(t, s, first) != "G":
                    return
                pool.wait_ge(zh_ready, count("VG", t, s, first))
                buf = at(t, p, s, NZ)
                pool.tensor_tensor(z_lo[:, buf, :, :], z[:, buf, :, :], z_hi[:, buf, :, :],
                                   ALU.subtract).then_inc(zl_pool, 1)

            def step(t, p=None, first=None):
                p = t % 2 if p is None else p
                for s in slots_of(t):
                    low_part(t, p, first, s)

            step(PLAIN)
            step(PLAIN + 1)
            with pool.Fori(PLAIN // 2 + 1, T // 2 - 1, 1) as i:
                step(2 * i, 0, False)
                step(2 * i + 1, 1, False)
            step(T - 2)
            step(T - 1)
            pool.wait_ge(staged, T)
            pool.memset(feat_a[:, :], 0.0).then_inc(feat_cleared, 1)

        @block.scalar
        def _(act):
            act.wait_ge(w_loaded, 16 * W_LOADS)
            for n in range(len(BATCHES)):
                act.wait_ge(w_turned, n + 1)
                width = BATCHES[n] * O
                if n == 0:
                    full, high = w0_sq[:, :], w0_sq_r[:, :]
                elif n == 1:
                    full, high = (w[:, :, :].rearrange("p a b -> p (a b)") for w in (w0_t, w0_hi))
                else:
                    full, high = (w[:, 4 * (n - 2):4 * (n - 1), :].rearrange("p a b -> p (a b)")
                                  for w in (w1_t, w1_hi))
                nc.scalar.copy(full, turned(n)[:, 0:width]).then_inc(w_copied, 1)
                nc.scalar.copy(high, turned(n)[:, 0:width]).then_inc(w_copied, 1)

            def stage_high(t):
                act.wait_ge(emb_ready, t // GPB + 1)
                if not isinstance(t, int) or t > 0:
                    act.wait_ge(transposed, t)
                src = emb[:, bass.ds((t // GPB) * F, F), bass.ds((t % GPB) * DPC, DPC)].rearrange("p f d -> p d f")
                nc.scalar.copy(stage[:, :, :, 0, :],
                               src.unsqueeze(2).to_broadcast([P, DPC, 2, F])).then_inc(hi_staged, 1)

            def copy_xhl0(t):
                act.wait_ge(transposed, t + 1)
                if not isinstance(t, int) or t > 0:
                    act.wait_ge(selected, pos(t - 2, S_L0_LAST) + 1)
                nc.scalar.copy(xhl0[:, :], p_x[:, :]).then_inc(xhl0_ready, 1)

            def copy_xhl1(t, p):
                act.wait_ge(xhl0_ready, t + 1)
                if not isinstance(t, int) or t > 1:
                    act.wait_ge(selected, pos(t - 2, NS - 1) + 1)
                nc.scalar.copy(xhl1[:, p, :], xhl0[:, :]).then_inc(xhl1_ready, 1)

            def copy_x4(t):
                act.wait_ge(quad_ready, t + 1)
                if not isinstance(t, int) or t > 0:
                    act.wait_ge(z_ready, pos(t - 2, S_L0_LAST) + 1)
                nc.scalar.copy(x4[:, :], p_x[:, :]).then_inc(x4_ready, 1)
                act.wait_ge(x4_ready, t + 1)
                nc.scalar.activation(p_x[:, :], p_x[:, :], ACT.Square).then_inc(squared, 1)

            def square_high(t):
                act.wait_ge(squared, 2 * t + 1)
                if not isinstance(t, int) or t > 0:
                    act.wait_ge(out0_ready, t)
                nc.scalar.copy(sq_r[:, :], p_x[:, :]).then_inc(squared, 1)

            def relu_out0(t, p):
                act.wait_ge(out0_ready, t + 1)
                if not isinstance(t, int) or t > 1:
                    act.wait_ge(z_ready, pos(t - 2, NS - 1) + 1)
                nc.scalar.activation(hid2[0:H, p, :], p_out0[0:H, :], ACT.Relu,
                                     bias=b0_sb[0:H, :]).then_inc(hid_ready, 1)
                nc.scalar.activation(hid2[H:P, p, :], p_out0[0:H, :], ACT.Relu,
                                     bias=b0_sb[0:H, :]).then_inc(hid_ready, 1)

            def relu_direct(t):
                if not isinstance(t, int) or t > 0:
                    act.wait_ge(direct_used, 2 * t)
                nc.scalar.activation(direct[H:P, :], p_out0[H:P, :], ACT.Relu,
                                     bias=b0_sb[H:P, :]).then_inc(direct_ready, 1)

            def relu_out1(t, p):
                act.wait_ge(contracted, pos(t, NS - 1) + 1)
                if not isinstance(t, int) or t > 1:
                    act.wait_ge(rel1_used, 2 * (t - 1))
                nc.scalar.activation(rel1[:, p, :], p_out1[:, p, :], ACT.Relu,
                                     bias=b1_sb[:, :]).then_inc(rel1_ready, 1)

            def high_part(t, p, first, s):
                if who(t, s, first) == "N":
                    return
                act.wait_ge(z_ready, pos(t, s) + 1)
                if not isinstance(t, int) or pos(t, s) >= NZ:
                    act.wait_ge(contracted, pos(t, s) + 1 - NZ)
                buf = at(t, p, s, NZ)
                nc.scalar.copy(z_hi[:, buf, :, :], z[:, buf, :, :]).then_inc(zh_ready, 1)

            def step(t, p=None, first=None):
                p = t % 2 if p is None else p
                for s in range(NS):
                    if s in slots_of(t):
                        high_part(t, p, first, s)
                    if s == 0 and has(t, 0):
                        relu_direct(t)
                    if s == S_SQUARE and has(t, 1):
                        square_high(t + 1)
                    if s == 2 and has(t, 1):
                        copy_xhl1(t + 1, 1 - p)
                    if s == S_STAGE and has(t, 2):
                        stage_high(t + 2)
                    if s == S_OUT1 and has(t, -1):
                        relu_out1(t - 1, 1 - p)
                    if s == S_TURN and has(t, 2):
                        copy_xhl0(t + 2)
                    if s == S_OUT0 + 1 and has(t, 1):
                        relu_out0(t + 1, 1 - p)
                    if s == S_QUAD + 1 and has(t, 2):
                        copy_x4(t + 2)

            steps(act, step)
            relu_out1(T - 1, (T - 1) % 2)

            done = 0
            act.wait_ge(top_loaded, 16 * TOP_LOADS)
            act.wait_ge(feat_cleared, 2)
            for half in range(2):
                act.wait_ge(dense_turned, half + 1)
                nc.scalar.copy(feat_a[0:DENSE, half * C:(half + 1) * C],
                               p_out0[0:DENSE, :] if half == 0 else p_x[0:DENSE, :]).then_inc(dense_ready, 1)
            for half in range(2):
                cols = slice(half * C, (half + 1) * C)
                for k in range(H1 // P):
                    done += 1
                    act.wait_ge(top_mm, done)
                    nc.scalar.activation(h1_sb[:, k, cols], top_bank(done - 1), ACT.Relu,
                                         bias=bt1_sb[:, k:k + 1]).then_inc(top_act, 1)
            for half in range(2):
                cols = slice(half * C, (half + 1) * C)
                for k in range(H2 // P):
                    done += 1
                    act.wait_ge(top_mm, done)
                    nc.scalar.activation(h2_sb[:, k, cols], top_bank(done - 1), ACT.Relu,
                                         bias=bt2_sb[:, k:k + 1]).then_inc(top_act, 1)
            for half in range(2):
                done += 1
                act.wait_ge(top_mm, done)
                nc.scalar.copy(y_sb[:, half * C:(half + 1) * C],
                               top_bank(done - 1)[0:1, :]).then_inc(top_act, 1)

        @block.vector
        def _(dve):
            nc.vector.memset(wt1a[:, :], 0.0).then_inc(feat_cleared, 1)
            dve.wait_ge(ident_ready, 2)
            nc.vector.tensor_copy(ident_r[:, :], ident[:, :])
            nc.vector.tensor_copy(sel_r[:, :, :], fold[:, 0:F].unsqueeze(2).to_broadcast([P, F, H]))
            for s in range(SHIFTS):
                nc.vector.tensor_copy(rot_r[:, s, :], fold[:, s + 1:s + 1 + F])
            nc.vector.tensor_copy(rep_r[:, :, :],
                                  fold[:, 0:F].unsqueeze(1).to_broadcast([P, 4, F])).then_inc(consts_ready, 1)
            dve.wait_ge(w_loaded, 16 * W_LOADS)
            v = w0_sb.rearrange("p (i j) -> p i j", j=F)
            nc.vector.tensor_tensor(w0_sym.rearrange("p (i j) -> p i j", j=F), v,
                                    w0_sb.rearrange("p (i j) -> p j i", j=F), ALU.add).then_inc(w0_added, 1)
            nc.vector.tensor_copy(w1_mh.rearrange("p (m h) -> p m h", h=H),
                                  w1_sb.rearrange("p (h m) -> p m h", m=F))
            for r in range(4):
                nc.vector.tensor_scalar(w0_diag[:, r, :], w0_sb[:, 0:F * F:F + 1], 1.0, None, ALU.mult)
            dve.wait_ge(w0_added, 1)
            for s in range(1, SHIFTS + 1):
                scale = 0.5 if s == SHIFTS else 1.0
                split = F - s
                nc.vector.tensor_scalar(w0_pair[:, s - 1, 0:split], w0_sym[:, s:s + (F + 1) * (split - 1) + 1:F + 1],
                                        scale, None, ALU.mult)
                start = (F + 1) * split + s - F
                last = nc.vector.tensor_scalar(w0_pair[:, s - 1, split:F],
                                               w0_sym[:, start:start + (F + 1) * (s - 1) + 1:F + 1],
                                               scale, None, ALU.mult)
            last.then_inc(w0_folded, 1)

            for n in range(len(BATCHES)):
                dve.wait_ge(w_copied, 2 * (n + 1))
                if n == 0:
                    for q in (1, 3):
                        rows = slice(q * F, (q + 1) * F)
                        last = nc.vector.tensor_tensor(w0_sq_r[rows, :], w0_sq[rows, :], w0_sq_r[rows, :],
                                                       ALU.subtract)
                elif n == 1:
                    last = nc.vector.tensor_tensor(w0_lo[:, :, :], w0_t[:, :, :], w0_hi[:, :, :], ALU.subtract)
                else:
                    k = slice(4 * (n - 2), 4 * (n - 1))
                    last = nc.vector.tensor_tensor(w1_lo[:, k, :], w1_t[:, k, :], w1_hi[:, k, :], ALU.subtract)
                last.then_inc(w_split, 1)

            def stage_low(t):
                dve.wait_ge(hi_staged, t + 1)
                src = emb[:, bass.ds((t // GPB) * F, F), bass.ds((t % GPB) * DPC, DPC)].rearrange("p f d -> p d f")
                nc.vector.tensor_tensor(stage[:, :, :, 1, :], src.unsqueeze(2).to_broadcast([P, DPC, 2, F]),
                                        stage[:, :, :, 0, :], ALU.subtract).then_inc(staged, 1)

            def squares_low(t):
                dve.wait_ge(squared, 2 * (t + 1))
                nc.vector.tensor_tensor(sq_r[H:P, :], p_x[H:P, :], sq_r[H:P, :], ALU.subtract).then_inc(sq_ready, 1)

            def multiply(t, p, first, s, other):
                g = pos(t, s)
                dve.wait_ge(selected, g + 1)
                if not isinstance(t, int) or g >= NZ:
                    dve.wait_ge(contracted, g + 1 - NZ)
                nc.vector.tensor_tensor(z[:, at(t, p, s, NZ), :, :], pair[at(t, p, s, 2)][:, :, :],
                                        other.unsqueeze(1).to_broadcast([P, 2, C]),
                                        ALU.mult).then_inc(z_ready, 1)

            def low_part(entry, a):
                if entry is None or who(entry[0], entry[3], entry[2]) != "V":
                    return
                t, p, first, s = entry
                dve.wait_ge(zh_ready, count("VG", t, s, first))
                buf = at(t, p, s, NZ)
                nc.vector.tensor_tensor(z_lo[:, buf, a, :], z[:, buf, a, :], z_hi[:, buf, a, :],
                                        ALU.subtract).then_inc(zl_vector, 1)

            def add_up(t, acc, src, used):
                for half in range(2):
                    if half or not isinstance(t, int) or t > 0:
                        dve.wait_ge(used, 2 * t + half)
                    dst = acc[:, bass.ds(t // GPB, 1), :]
                    nc.vector.tensor_tensor(dst, dst, src[:, half * (C // 2):(half + 1) * (C // 2)].unsqueeze(1),
                                            ALU.add).then_inc(used, 1)

            def add_direct(t):
                dve.wait_ge(direct_ready, t + 1)
                add_up(t, acc0[H:P, :, :], direct[H:P, :], direct_used)

            def add_rel1(t, p):
                dve.wait_ge(rel1_ready, t + 1)
                add_up(t, acc1[:, :, :], rel1[:, p, :], rel1_used)

            dve.wait_ge(w_turned, len(BATCHES))
            nc.vector.memset(acc0[:, :, :], 0.0).then_inc(acc_cleared, 1)
            nc.vector.memset(acc1[:, :, :], 0.0).then_inc(acc_cleared, 1)
            dve.wait_ge(acc_cleared, 2)

            def step(t, p=None, first=None):
                p = t % 2 if p is None else p
                slots = slots_of(t)
                for s in range(NS):
                    if s in slots:
                        kind, k = SLOTS[s]
                        if (kind, k) == ("L1", 0):
                            dve.wait_ge(hid_ready, 2 * (t + 1))
                        if (kind, k) == ("L0", 0):
                            dve.wait_ge(x4_ready, t + 2)
                        multiply(t, p, first, s, x4[:, :] if kind == "L0" else hid2[:, p, :])
                        for a in (1, 0):
                            low_part(lagged(t, p, first, slots.index(s), LOW_LAG + a), a)
                    if s == S_SQUARE + 3 and has(t, 1):
                        squares_low(t + 1)
                    if s == S_STAGE + 2 and has(t, 2):
                        stage_low(t + 2)
                    if s == 8 and has(t, 0):
                        add_direct(t)
                    if s == 9 and has(t, -1):
                        add_rel1(t - 1, 1 - p)
                if isinstance(t, int):
                    left = rest(t, LOW_LAG + 1)
                    for i, entry in enumerate(left):
                        for a in range(2):
                            if a == 1 or len(left) <= LOW_LAG or i > 0:
                                low_part(entry, a)

            steps(dve, step)
            def dim_sums(dst, acc, rows, groups):
                nc.vector.tensor_reduce(dst[rows, groups.start * P:groups.stop * P].rearrange("p (c b) -> p c b", b=P),
                                        acc[rows, groups, :].rearrange("p c (d b) -> p c b d", b=P),
                                        AX.X, ALU.add).then_inc(feat_ready, 1)

            dve.wait_ge(feat_cleared, 2)
            dve.wait_ge(direct_used, 2 * T)
            dim_sums(feat_a, acc0, slice(H, P), slice(0, BC))
            dve.wait_ge(rel1_used, 2 * (T - 1))
            dim_sums(feat_b, acc1, slice(0, P), slice(0, BC // 2))
            add_rel1(T - 1, (T - 1) % 2)
            dve.wait_ge(rel1_used, 2 * T)
            dim_sums(feat_b, acc1, slice(0, P), slice(BC // 2, BC))

        @block.tensor
        def _(pe):
            pe.wait_ge(ident_ready, 1)
            pe.wait_ge(w0_folded, 1)
            for n, batch in enumerate(BATCHES):
                if n >= 2:
                    pe.wait_ge(w_copied, 2 * (n - 1))
                for a in range(batch):
                    if n == 0:
                        src = w0_diag.rearrange("p r i -> p (r i)")
                    elif n == 1:
                        src = w0_pair[:, 4 * a:4 * a + 4, :].rearrange("p s i -> p (s i)")
                    else:
                        j = 4 * (n - 2) + a
                        src = w1_mh[:, j * P:(j + 1) * P]
                    last = nc.tensor.transpose(turned(n)[:, a * O:(a + 1) * O], src, ident[:, :])
                last.then_inc(w_turned, 1)
            pe.wait_ge(w_copied, 2 * len(BATCHES))
            pe.wait_ge(w_split, len(BATCHES))
            pe.wait_ge(consts_ready, 1)

            def transpose_chunk(t):
                pe.wait_ge(staged, t + 1)
                if not isinstance(t, int) or t > 0:
                    pe.wait_ge(sq_ready, t)
                for d in range(DPC):
                    last = nc.tensor.matmul(p_x[:, d * P:(d + 1) * P], stage[:, d, :, :, :].rearrange("p c l f -> p (c l f)"), ident_r[:, :],
                                            start=True, stop=True)
                last.then_inc(transposed, 1)

            def quadruple(t):
                pe.wait_ge(xhl0_ready, t + 1)
                nc.tensor.matmul(p_x[:, :], rep_r[0:2 * F, :, :].rearrange("p r i -> p (r i)"), xhl0[0:2 * F, :],
                                 start=True, stop=True).then_inc(quad_ready, 1)

            def select(t, p, first, s):
                kind, k = SLOTS[s]
                g = pos(t, s)
                x = xhl1[:, p, :] if kind == "L1" else xhl0[:, :]
                if (kind, k) == ("L1", 0):
                    pe.wait_ge(xhl1_ready, t + 1)
                if not isinstance(t, int) or g >= 2:
                    pe.wait_ge(z_ready, g - 1)
                for a in range(2):
                    rows = slice(a * 2 * F, (a + 1) * 2 * F)
                    j = 2 * k + a
                    pick = (sel_r[rows, 2 * j:2 * j + 2, :] if kind == "L1" else rot_r[rows, 4 * j:4 * j + 4, :]
                            ).rearrange("p a b -> p (a b)")
                    last = nc.tensor.matmul(pair[at(t, p, s, 2)][:, a, :], pick, x[rows, :],
                                            start=True, stop=True)
                last.then_inc(selected, 1)

            def squares(t):
                pe.wait_ge(sq_ready, t + 1)
                nc.tensor.matmul(p_out0[:, :], w0_sq_r[:, :], sq_r[:, :], start=False,
                                 stop=True).then_inc(out0_ready, 1)

            def contract(entry):
                if entry is None:
                    return
                t, p, first, s = entry
                kind, k = SLOTS[s]
                if (kind, k) == ("L0", 0) and (not isinstance(t, int) or t >= 0):
                    pe.wait_ge(direct_ready, t + 1)
                if (kind, k) == ("L1", 0) and (not isinstance(t, int) or t > 1):
                    pe.wait_ge(rel1_ready, t - 1)
                maker = who(t, s, first)
                if maker == "N":
                    pe.wait_ge(z_ready, pos(t, s) + 1)
                else:
                    pe.wait_ge(zh_ready, count("VG", t, s, first))
                buf = at(t, p, s, NZ)
                full, high, low = (w1_t, w1_hi, w1_lo) if kind == "L1" else (w0_t, w0_hi, w0_lo)
                dst = p_out1[:, p, :] if kind == "L1" else p_out0[:, :]
                tiles = F // 2 if kind == "L1" else SHIFTS // 4
                work = []
                for a in range(2):
                    j = 2 * k + a
                    if maker == "N":
                        work.append((full[:, j, :], z[:, buf, a, :], a, False))
                    else:
                        work += [(w[:, j, :], z_hi[:, buf, a, :], a, False) for w in (high, low)]
                if maker != "N":
                    work += [(high[:, 2 * k + a, :], z_lo[:, buf, a, :], a, True) for a in range(2)]
                for i, (w, x, a, x_low) in enumerate(work):
                    if maker == "V" and x_low:
                        pe.wait_ge(zl_vector, 2 * count("V", t, s, first) - 1 + a)
                    if maker == "G" and x_low and a == 0:
                        pe.wait_ge(zl_pool, count("G", t, s, first))
                    last = nc.tensor.matmul(dst, w, x, start=(k == 0 and i == 0),
                                            stop=(kind == "L1" and 2 * k + 2 == tiles and i == len(work) - 1))
                last.then_inc(contracted, 1)
                if (kind, k) == ("L0", 1):
                    squares(t + 1)

            def step(t, p=None, first=None):
                p = t % 2 if p is None else p
                slots = slots_of(t)
                for s in range(NS):
                    if s in slots:
                        select(t, p, first, s)
                        contract(lagged(t, p, first, slots.index(s), LAG))
                    if s == S_TURN and has(t, 2):
                        transpose_chunk(t + 2)
                    if s == S_QUAD and has(t, 2):
                        quadruple(t + 2)
                for entry in rest(t, LAG) if isinstance(t, int) else []:
                    contract(entry)

            steps(pe, step)

            pe.wait_ge(top_loaded, 16 * TOP_LOADS)
            pe.wait_ge(direct_ready, T)
            pe.wait_ge(sq_ready, T)
            for c in range(BC):
                bank = p_out0 if c < 4 else p_x
                last = nc.tensor.transpose(bank[0:DENSE, (c % 4) * P:(c % 4 + 1) * P], dense_sb[:, c, :], ident[:, :])
                if c % 4 == 3:
                    last.then_inc(dense_turned, 1)
            done = 0
            for half in range(2):
                pe.wait_ge(feat_ready, 2 + half)
                pe.wait_ge(dense_ready, half + 1)
                cols = slice(half * C, (half + 1) * C)
                for k in range(H1 // P):
                    if done >= 4:
                        pe.wait_ge(top_act, done - 3)
                    nc.tensor.matmul(top_bank(done), wt1a[:, k * P:(k + 1) * P], feat_a[:, cols], start=True, stop=False)
                    nc.tensor.matmul(top_bank(done), wt1b[:, k * P:(k + 1) * P], feat_b[:, cols], start=False,
                                     stop=True).then_inc(top_mm, 1)
                    done += 1
            for half in range(2):
                cols = slice(half * C, (half + 1) * C)
                for k in range(H2 // P):
                    pe.wait_ge(top_act, max(done - 3, 4 * (half + 1)))
                    for q in range(H1 // P):
                        last = nc.tensor.matmul(top_bank(done), wt2_sb[:, q, k * P:(k + 1) * P], h1_sb[:, q, cols],
                                                start=(q == 0), stop=(q == H1 // P - 1))
                    last.then_inc(top_mm, 1)
                    done += 1
            for half in range(2):
                cols = slice(half * C, (half + 1) * C)
                pe.wait_ge(top_act, max(done - 3, 8 + 2 * (half + 1)))
                for q in range(H2 // P):
                    last = nc.tensor.matmul(top_bank(done)[0:1, :], wt3_sb[:, q:q + 1], h2_sb[:, q, cols],
                                            start=(q == 0), stop=(q == H2 // P - 1))
                last.then_inc(top_mm, 1)
                done += 1


_FIRST = ["dense_ctx", "ids"]
_TABLES = [f"tbl_{i}" for i in range(F)]
_REST = ["L0_rec_W0", "L0_rec_b0", "L0_rec_W1", "L0_rec_b1", "W_top1", "b_top1", "W_top2", "b_top2", "W_top3"]


def kernel(**inputs):
    import numpy as np
    import concourse.bacc as bacc
    from concourse.bass_utils import run_bass_kernel_spmd

    nc = bacc.Bacc("TRN2", target_bir_lowering=False, num_devices=1)
    arrays, aps = {}, {}
    for name in _FIRST + _TABLES + _REST:
        a = np.ascontiguousarray(inputs[name])
        arrays[f"in_{name}"] = a
        aps[name] = nc.dram_tensor(f"in_{name}", a.shape, mybir.dt.from_np(a.dtype), kind="ExternalInput").ap()
    out = nc.dram_tensor("out_y", (B, 1), F32, kind="ExternalOutput").ap()
    cin_tower(nc, aps["dense_ctx"], aps["ids"], [aps[n] for n in _TABLES], *[aps[n] for n in _REST], out)
    return run_bass_kernel_spmd(nc, [arrays], core_ids=[0]).results[0]["out_y"]
```

```python
from contextlib import ExitStack

import concourse.bass as bass
from concourse import mybir

F32 = mybir.dt.float32
F32R = mybir.dt.float32r
I32 = mybir.dt.int32
ALU = mybir.AluOpType
ACT = mybir.ActivationFunctionType
AX = mybir.AxisListType

P = 128
B = 1024
F = 32
D = 64
O = 128
H = O // 2
DENSE = 16
H1, H2 = 512, 256
BC = B // P
DPC = 4
C = DPC * P
GPB = D // DPC
T = BC * GPB
SHIFTS = F // 2

SLOTS = [("L1", 0), ("L0", 0), ("L0", 1), ("L1", 1), ("L1", 2),
         ("L1", 3), ("L1", 4), ("L1", 5), ("L1", 6), ("L1", 7)]
NS = len(SLOTS)
LAG = 4
LOW_LAG = 2
NZ = 5
PLAIN = 12
LATE = 5
WHO_FIRST = "VNVNVNVNVN"
WHO = "GVGGGVGGVG"

SPREAD = tuple(SLOTS.index(("L1", k)) for k in range(3))
SPREAD_FROM = PLAIN + 2
SPREAD_DMAS = 2
ROWS_SPREAD = 4 * len(SPREAD)

S_SQUARE = 1
S_STAGE = 3
S_STAGE_LOW = 2
S_COPY_LOW = 4
S_TURN = 6
S_QUAD = 8
S_OUT1 = LAG - 1
S_L0_LAST = SLOTS.index(("L0", 1))
S_OUT0 = S_L0_LAST + LAG


def slots_of(t):
    if isinstance(t, int) and t < -1:
        return []
    if isinstance(t, int) and t < 0:
        return [s for s in range(NS) if SLOTS[s][0] == "L0"]
    if isinstance(t, int) and t == T - 1:
        return [s for s in range(NS) if SLOTS[s][0] == "L1"]
    return list(range(NS))


def who(t, s, first):
    return (WHO_FIRST if (t < PLAIN if isinstance(t, int) else first) else WHO)[s]


def spread(t, s, first):
    return s in SPREAD and (t >= SPREAD_FROM if isinstance(t, int) else not first)


def count(which, t, s, first):
    if isinstance(t, int):
        return sum(who(u, v, None) in which for u in range(-1, t + 1) for v in slots_of(u) if u < t or v <= s)
    t0 = 0 if first else PLAIN
    each = sum(w in which for w in (WHO_FIRST if first else WHO))
    return t * each + (count(which, t0, s, None) - t0 * each)


def cin_tower(nc, dense, ids, tables, w0, b0, w1, b1, wt1, bt1, wt2, bt2, wt3, x_rows, out):
    ctx = ExitStack()
    with ctx:
        def sb(name, shape, dt=F32):
            return ctx.enter_context(nc.sbuf_tensor(name, shape, dt))

        def ps(name, shape):
            return ctx.enter_context(nc.psum_tensor(name, shape, F32))

        def sem(name):
            return ctx.enter_context(nc.semaphore(name))


        emb = sb("emb", [P, BC * F, D])
        w0_words = SHIFTS // 4 * O
        early = sb("early", [P, w0_words + O + P + BC * F])
        w0_t = early[:, 0:w0_words].rearrange("p (k o) -> p k o", o=O)
        w0_sq = early[:, w0_words:w0_words + O]
        ident = early[:, w0_words + O:w0_words + O + P]
        ids_sb = early[:, w0_words + O + P:].rearrange("p (c f) -> p c f", f=F).bitcast(I32)
        stage = sb("stage", [P, DPC, 2, 2, F], F32R)
        xhl0 = sb("xhl0", [P, C], F32R)
        xhl1 = sb("xhl1", [P, 2, C], F32R)
        x4 = sb("x4", [P, C])
        sq_r = sb("sq_r", [P, C], F32R)
        z = sb("z", [P, NZ, 2, C])
        z_hi = sb("z_hi", [P, NZ, 2, C], F32R)
        z_lo = sb("z_lo", [P, NZ, 2, C], F32R)
        hid2 = sb("hid2", [P, 2, C])
        direct = sb("direct", [P, C])
        rel1 = sb("rel1", [P, 2, C])
        acc0 = sb("acc0", [P, BC, C // 2])
        acc1 = sb("acc1", [P, BC, C // 2])
        ident_r = sb("ident_r", [P, P], F32R)
        sel_r = sb("sel_r", [P, F, H], F32R)
        rot_r = sb("rot_r", [P, SHIFTS, F], F32R)
        rep_r = sb("rep_r", [P, 4, F], F32R)
        w0_hi = sb("w0_hi", [P, SHIFTS // 4, O], F32R)
        w0_lo = sb("w0_lo", [P, SHIFTS // 4, O], F32R)
        w1_hi = sb("w1_hi", [P, F // 2, O], F32R)
        w1_lo = sb("w1_lo", [P, F // 2, O], F32R)
        w0_sq_r = sb("w0_sq_r", [P, O], F32R)
        w1_t = sb("w1_t", [P, F // 2, O])
        b0_sb = sb("b0_sb", [P, 1])
        b1_sb = sb("b1_sb", [P, 1])
        wt3_sb = sb("wt3_sb", [P, H2 // P])
        bt1_sb = sb("bt1_sb", [P, H1 // P])
        bt2_sb = sb("bt2_sb", [P, H2 // P])
        wt1a = sb("wt1a", [P, H1])
        scr = z[:, :, :, :].rearrange("p a b c -> p (a b c)")
        w0_sb, w0_sym = scr[:, 0:F * F], scr[:, F * F:2 * F * F]
        w0_pair = scr[:, 2 * F * F:2 * F * F + SHIFTS * F].rearrange("p (s i) -> p s i", i=F)
        w0_diag = scr[:, 3 * F * F:3 * F * F + P].rearrange("p (r i) -> p r i", i=F)
        fold = scr[:, 4 * F * F:4 * F * F + 2 * F]
        w1_sb = acc1[:, :, :].rearrange("p a b -> p (a b)")
        w1_mh = acc0[:, :, :].rearrange("p a b -> p (a b)")
        w1_t_flat = w1_t[:, :, :].rearrange("p a b -> p (a b)")
        x_spread = [part.rearrange("p (a c) -> p a c", c=C)
                    for part in (w1_t_flat[:, 0:2 * C], w1_t_flat[:, 2 * C:4 * C], early[:, :])]
        top = emb[:, :, :].rearrange("p a d -> p (a d)")
        feat_a, feat_b = top[:, 0:B], top[:, B:2 * B]
        h1_sb = top[:, 2 * B:2 * B + 4 * B].rearrange("p (k b) -> p k b", b=B)
        h2_sb = top[:, 6 * B:8 * B].rearrange("p (k b) -> p k b", b=B)
        y_sb = top[0:1, 8 * B:9 * B]
        odd_feat = top[:, 9 * B:10 * B]
        off = LATE * F * D
        wt1b = top[:, off:off + H1]
        off += H1
        wt2_sb = top[:, off:off + H1 // P * H2].rearrange("p (k n) -> p k n", n=H2)
        off += H1 // P * H2
        dense_sb = top[:, off:off + BC * DENSE].rearrange("p (c f) -> p c f", f=DENSE)
        off += BC * DENSE
        late_ident = top[:, off:off + P]

        pair = [ps(f"pair{i}", [P, 2, C]) for i in range(2)]
        p_out1 = ps("p_out1", [P, 2, C])
        p_out0 = ps("p_out0", [P, C])
        p_x = ps("p_x", [P, C])

        ids_loaded = sem("ids_loaded")
        w_loaded = sem("w_loaded")
        top_loaded = sem("top_loaded")
        gathered = [sem(f"gathered{i}") for i in range(BC)]
        emb_ready = sem("emb_ready")
        pool_made = sem("pool_made")
        ident_ready = sem("ident_ready")
        consts_ready = sem("consts_ready")
        w0_added = sem("w0_added")
        w0_folded = sem("w0_folded")
        w_turned = sem("w_turned")
        w_copied = sem("w_copied")
        acc_cleared = sem("acc_cleared")
        hi_staged = sem("hi_staged")
        low_staged = sem("low_staged")
        w_split = sem("w_split")
        sq_ready = sem("sq_ready")
        zh_ready = sem("zh_ready")
        zl_vector = sem("zl_vector")
        zl_pool = sem("zl_pool")
        staged = sem("staged")
        transposed = sem("transposed")
        xhl0_ready = sem("xhl0_ready")
        xhl1_ready = sem("xhl1_ready")
        squared = sem("squared")
        quad_ready = sem("quad_ready")
        x4_ready = sem("x4_ready")
        x_rows_stored = sem("x_rows_stored")
        x_spread_loaded = [sem(f"x_spread_loaded{i}") for i in range(len(SPREAD))]
        selected = sem("selected")
        z_ready = sem("z_ready")
        contracted = sem("contracted")
        out0_ready = sem("out0_ready")
        hid_ready = sem("hid_ready")
        direct_ready = sem("direct_ready")
        direct_used = sem("direct_used")
        rel1_ready = sem("rel1_ready")
        rel1_used = sem("rel1_used")
        odd_summed = sem("odd_summed")
        late_ident_ready = sem("late_ident_ready")
        dense_turned = sem("dense_turned")
        feat_cleared = sem("feat_cleared")
        feat_ready = sem("feat_ready")
        dense_ready = sem("dense_ready")
        top_mm = sem("top_mm")
        top_act = sem("top_act")
        stored = sem("stored")

        block = ctx.enter_context(nc.Block())

        def steps(eng, step):
            for t in (-2, -1, 0, 1):
                step(t)
            with eng.Fori(1, PLAIN // 2, 1) as i:
                step(2 * i, 0, True)
                step(2 * i + 1, 1, True)
            step(PLAIN)
            step(PLAIN + 1)
            with eng.Fori(PLAIN // 2 + 1, T // 2 - 1, 1) as i:
                step(2 * i, 0, False)
                step(2 * i + 1, 1, False)
            step(T - 2)
            step(T - 1)

        def has(t, k):
            return not isinstance(t, int) or 0 <= t + k < T

        BATCHES = [1, 4, 4, 4, 4, 4]
        TOP_ACTS = 2 * (H1 // P) + 2 * (H2 // P) + 2

        def turned(n):
            return pair[n % 2][:, 0, :]

        TOP_BANKS = [pair[0][:, 0, :], pair[0][:, 1, :], pair[1][:, 0, :], pair[1][:, 1, :]]

        def top_bank(n):
            return TOP_BANKS[n % 4]

        def pos(t, s):
            if isinstance(t, int):
                return count("NVG", t, s, None) - 1
            return t * NS + (pos(0, s))

        def at(t, p, s, n):
            return pos(t, s) % n if isinstance(t, int) else (p * NS + pos(0, s)) % n

        def lagged(t, p, first, n, lag):
            slots = slots_of(t)
            if n >= lag:
                return t, p, first, slots[n - lag]
            if isinstance(t, int) and t < 1:
                before = [(u, u % 2, None, s) for u in range(0, t) for s in slots_of(u)]
                k = len(before) - lag + n
                return before[k] if k >= 0 else None
            return t - 1, 1 - p, first, NS - lag + n

        def rest(t, lag):
            return [(t, t % 2, None, s) for s in slots_of(t)[-lag:]] if t in (-1, T - 1) else []

        W_LOADS = 4
        TOP_LOADS = 8

        def stage_low(eng, t):
            eng.wait_ge(hi_staged, t + 1)
            src = emb[:, bass.ds((t // GPB) * F, F), bass.ds((t % GPB) * DPC, DPC)].rearrange("p f d -> p d f")
            eng.tensor_tensor(stage[:, :, 0, 1, :], src, stage[:, :, 0, 0, :], ALU.subtract).then_inc(low_staged, 1)

        @block.sync
        def _(sp):
            sp.dma_start(ids_sb[:, :, :], ids.rearrange("(c p) f -> p c f", p=P)).then_inc(ids_loaded, 16)
            sp.dma_start(w0_sb, w0).then_inc(w_loaded, 16)
            sp.dma_start(w1_sb, w1).then_inc(w_loaded, 16)
            sp.dma_start(b0_sb[:, :], b0.rearrange("(p a) -> p a", a=1)).then_inc(w_loaded, 16)
            sp.dma_start(b1_sb[:, :], b1.rearrange("(p a) -> p a", a=1)).then_inc(w_loaded, 16)
            sp.wait_ge(feat_cleared, 1)
            sp.dma_start(wt1a[0:DENSE, :], wt1[O + H:O + H + DENSE, :]).then_inc(top_loaded, 16)
            sp.dma_start(wt1a[H:P, :], wt1[0:H, :]).then_inc(top_loaded, 16)
            sp.dma_start(wt3_sb[:, :], wt3.rearrange("(k p) n -> p (k n)", p=P),
                         allow_slow_non_contiguous=True).then_inc(top_loaded, 16)
            sp.dma_start(bt1_sb[:, :], bt1.rearrange("(k p) -> p k", p=P),
                         allow_slow_non_contiguous=True).then_inc(top_loaded, 16)
            sp.dma_start(bt2_sb[:, :], bt2.rearrange("(k p) -> p k", p=P),
                         allow_slow_non_contiguous=True).then_inc(top_loaded, 16)

            def load_spread(t):
                n = t - SPREAD_FROM
                sp.wait_ge(x4_ready, t + 1)
                if not isinstance(t, int):
                    for loaded in x_spread_loaded:
                        sp.wait_ge(loaded, 16 * SPREAD_DMAS * n)
                sp.dma_start(x_rows, x4[0:ROWS_SPREAD, :]).then_inc(x_rows_stored, 16)
                sp.wait_ge(x_rows_stored, 16 * (n + 1))
                if isinstance(t, int):
                    sp.wait_ge(contracted, pos(PLAIN - 1, NS - 1) + 1)
                    sp.wait_ge(emb_ready, BC)
                for i, s in enumerate(SPREAD):
                    if not isinstance(t, int):
                        sp.wait_ge(z_ready, pos(t - 1, s) + 1)
                    fields = x_rows[4 * i:4 * i + 4, :].rearrange("(a h) c -> h a c", h=2)
                    for h in range(SPREAD_DMAS):
                        sp.dma_start(x_spread[i][h * H:(h + 1) * H, :, :],
                                     fields[h, :, :].partition_broadcast(H)).then_inc(x_spread_loaded[i], 16)

            load_spread(SPREAD_FROM)
            with sp.Fori(SPREAD_FROM + 1, T, 1) as t:
                load_spread(t)
            sp.wait_ge(staged, (LATE + 1) * GPB)
            sp.dma_start(wt1b[:, :], wt1[H:H + O, :]).then_inc(top_loaded, 16)
            sp.dma_start(wt2_sb[:, :, :], wt2.rearrange("(k p) n -> p k n", p=P)).then_inc(top_loaded, 16)
            sp.dma_start(dense_sb[:, :, :], dense.rearrange("(c p) f -> p c f", p=P)).then_inc(top_loaded, 16)
            sp.wait_ge(top_act, TOP_ACTS)
            sp.dma_start(out.rearrange("b a -> a b"), y_sb).then_inc(stored, 16)
            sp.wait_ge(stored, 16)

        @block.gpsimd
        def _(pool):
            def gather(c, fields):
                for f in fields:
                    pool.indirect_dma_start(
                        emb[:, c * F + f, :], None, tables[f],
                        bass.IndirectOffsetOnAxis(ap=ids_sb[:, c, f:f + 1], axis=0),
                    ).then_inc(gathered[c], 16)

            EARLY = 3
            made = [0]

            def after(ins):
                made[0] += 1
                ins.then_inc(pool_made, 1)
                pool.wait_ge(pool_made, made[0])

            def identity(dst):
                after(pool.memset(dst, 0.0))
                return pool.affine_select(out=dst, in_=dst, compare_op=ALU.not_equal, fill=1.0, base=0,
                                          pattern=[[-1, P]], channel_multiplier=1)

            identity(ident).then_inc(ident_ready, 1)
            after(pool.memset(fold[:, :], 0.0))
            for base in range(F, -P, -F):
                after(pool.affine_select(out=fold[:, :], in_=fold[:, :], compare_op=ALU.not_equal, fill=1.0,
                                         base=base, pattern=[[-1, 2 * F]], channel_multiplier=1))
            pool.tensor_copy(fold[:, 0:1], fold[:, 0:1]).then_inc(ident_ready, 1)
            pool.wait_ge(ids_loaded, 16)
            gather(0, range(F))
            for c in range(BC):
                if c + 1 < BC:
                    gather(c + 1, range(EARLY))
                pool.wait_ge(gathered[c], 16 * F)
                pool.sem_inc(emb_ready, 1)
                if c + 1 < BC:
                    gather(c + 1, range(EARLY, F))

            def low_part(t, p, first, s):
                if who(t, s, first) != "G":
                    return
                pool.wait_ge(zh_ready, count("VG", t, s, first))
                buf = at(t, p, s, NZ)
                pool.tensor_tensor(z_lo[:, buf, :, :], z[:, buf, :, :], z_hi[:, buf, :, :],
                                   ALU.subtract).then_inc(zl_pool, 1)

            def step(t, p=None, first=None):
                p = t % 2 if p is None else p
                for s in range(NS):
                    if s in slots_of(t):
                        low_part(t, p, first, s)
                    if s == S_STAGE_LOW and has(t, 2):
                        stage_low(pool, t + 2)

            step(PLAIN)
            step(PLAIN + 1)
            with pool.Fori(PLAIN // 2 + 1, T // 2 - 1, 1) as i:
                step(2 * i, 0, False)
                step(2 * i + 1, 1, False)
            pool.wait_ge(staged, GPB)
            pool.memset(feat_a[:, :], 0.0).then_inc(feat_cleared, 1)
            pool.wait_ge(staged, (LATE + 1) * GPB)
            identity(late_ident).then_inc(late_ident_ready, 1)
            step(T - 2)
            step(T - 1)

        @block.scalar
        def _(act):
            act.wait_ge(w_loaded, 16 * W_LOADS)
            for n in range(len(BATCHES)):
                act.wait_ge(w_turned, n + 1)
                width = BATCHES[n] * O
                if n == 0:
                    full, high = w0_sq[:, :], w0_sq_r[:, :]
                elif n == 1:
                    full, high = (w[:, :, :].rearrange("p a b -> p (a b)") for w in (w0_t, w0_hi))
                else:
                    full, high = (w[:, 4 * (n - 2):4 * (n - 1), :].rearrange("p a b -> p (a b)")
                                  for w in (w1_t, w1_hi))
                nc.scalar.copy(full, turned(n)[:, 0:width]).then_inc(w_copied, 1)
                nc.scalar.copy(high, turned(n)[:, 0:width]).then_inc(w_copied, 1)

            def stage_high(t):
                act.wait_ge(emb_ready, t // GPB + 1)
                if not isinstance(t, int) or t > 0:
                    act.wait_ge(transposed, t)
                src = emb[:, bass.ds((t // GPB) * F, F), bass.ds((t % GPB) * DPC, DPC)].rearrange("p f d -> p d f")
                nc.scalar.copy(stage[:, :, :, 0, :],
                               src.unsqueeze(2).to_broadcast([P, DPC, 2, F])).then_inc(hi_staged, 1)

            def copy_low(t):
                act.wait_ge(low_staged, t + 1)
                nc.scalar.copy(stage[:, :, 1, 1, :], stage[:, :, 0, 1, :]).then_inc(staged, 1)

            def copy_xhl0(t):
                act.wait_ge(transposed, t + 1)
                if not isinstance(t, int) or t > 0:
                    act.wait_ge(selected, pos(t - 2, S_L0_LAST) + 1)
                nc.scalar.copy(xhl0[:, :], p_x[:, :]).then_inc(xhl0_ready, 1)

            def copy_xhl1(t, p):
                act.wait_ge(xhl0_ready, t + 1)
                if not isinstance(t, int) or t > 1:
                    act.wait_ge(selected, pos(t - 2, NS - 1) + 1)
                nc.scalar.copy(xhl1[:, p, :], xhl0[:, :]).then_inc(xhl1_ready, 1)

            def copy_x4(t, first):
                act.wait_ge(quad_ready, t + 1)
                if not isinstance(t, int) or t > 0:
                    act.wait_ge(z_ready, pos(t - 2, S_L0_LAST) + 1)
                if spread(t - 1, 0, first):
                    act.wait_ge(x_rows_stored, 16 * (t - SPREAD_FROM))
                nc.scalar.copy(x4[:, :], p_x[:, :]).then_inc(x4_ready, 1)
                act.wait_ge(x4_ready, t + 1)
                nc.scalar.activation(p_x[:, :], p_x[:, :], ACT.Square).then_inc(squared, 1)

            def square_high(t):
                act.wait_ge(squared, 2 * t + 1)
                if not isinstance(t, int) or t > 0:
                    act.wait_ge(out0_ready, t)
                nc.scalar.copy(sq_r[:, :], p_x[:, :]).then_inc(squared, 1)

            def relu_out0(t, p):
                act.wait_ge(out0_ready, t + 1)
                if not isinstance(t, int) or t > 1:
                    act.wait_ge(z_ready, pos(t - 2, NS - 1) + 1)
                nc.scalar.activation(hid2[0:H, p, :], p_out0[0:H, :], ACT.Relu,
                                     bias=b0_sb[0:H, :]).then_inc(hid_ready, 1)
                nc.scalar.activation(hid2[H:P, p, :], p_out0[0:H, :], ACT.Relu,
                                     bias=b0_sb[0:H, :]).then_inc(hid_ready, 1)

            def relu_direct(t, p):
                if not isinstance(t, int) or t > 1:
                    act.wait_ge(direct_used, t - p)
                rows = slice(0, H) if p else slice(H, P)
                nc.scalar.activation(direct[rows, :], p_out0[H:P, :], ACT.Relu,
                                     bias=b0_sb[H:P, :]).then_inc(direct_ready, 1)

            def relu_out1(t, p):
                act.wait_ge(contracted, pos(t, NS - 1) + 1)
                if not isinstance(t, int) or t > 1:
                    act.wait_ge(rel1_used, 2 * (t - 1))
                nc.scalar.activation(rel1[:, p, :], p_out1[:, p, :], ACT.Relu,
                                     bias=b1_sb[:, :]).then_inc(rel1_ready, 1)

            def high_part(t, p, first, s):
                if who(t, s, first) == "N":
                    return
                act.wait_ge(z_ready, pos(t, s) + 1)
                if not isinstance(t, int) or pos(t, s) >= NZ:
                    act.wait_ge(contracted, pos(t, s) + 1 - NZ)
                buf = at(t, p, s, NZ)
                nc.scalar.copy(z_hi[:, buf, :, :], z[:, buf, :, :]).then_inc(zh_ready, 1)

            def step(t, p=None, first=None):
                p = t % 2 if p is None else p
                for s in range(NS):
                    if s in slots_of(t):
                        high_part(t, p, first, s)
                    if s == 0 and has(t, 0):
                        relu_direct(t, p)
                    if s == S_SQUARE and has(t, 1):
                        square_high(t + 1)
                    if s == 2 and has(t, 1):
                        copy_xhl1(t + 1, 1 - p)
                    if s == S_STAGE and has(t, 2):
                        stage_high(t + 2)
                    if s == S_OUT1 and has(t, -1):
                        relu_out1(t - 1, 1 - p)
                    if s == S_COPY_LOW and has(t, 2):
                        copy_low(t + 2)
                    if s == S_TURN and has(t, 2):
                        copy_xhl0(t + 2)
                    if s == S_OUT0 + 1 and has(t, 1):
                        relu_out0(t + 1, 1 - p)
                    if s == S_QUAD + 1 and has(t, 2):
                        copy_x4(t + 2, first)

            steps(act, step)
            relu_out1(T - 1, (T - 1) % 2)

            done = 0
            act.wait_ge(top_loaded, 16 * TOP_LOADS)
            act.wait_ge(feat_cleared, 2)
            for half in range(2):
                act.wait_ge(dense_turned, half + 1)
                nc.scalar.copy(feat_a[0:DENSE, half * C:(half + 1) * C],
                               p_out0[0:DENSE, :] if half == 0 else p_x[0:DENSE, :]).then_inc(dense_ready, 1)
            for half in range(2):
                cols = slice(half * C, (half + 1) * C)
                for k in range(H1 // P):
                    done += 1
                    act.wait_ge(top_mm, done)
                    nc.scalar.activation(h1_sb[:, k, cols], top_bank(done - 1), ACT.Relu,
                                         bias=bt1_sb[:, k:k + 1]).then_inc(top_act, 1)
            for half in range(2):
                cols = slice(half * C, (half + 1) * C)
                for k in range(H2 // P):
                    done += 1
                    act.wait_ge(top_mm, done)
                    nc.scalar.activation(h2_sb[:, k, cols], top_bank(done - 1), ACT.Relu,
                                         bias=bt2_sb[:, k:k + 1]).then_inc(top_act, 1)
            for half in range(2):
                done += 1
                act.wait_ge(top_mm, done)
                nc.scalar.copy(y_sb[:, half * C:(half + 1) * C],
                               top_bank(done - 1)[0:1, :]).then_inc(top_act, 1)

        EARLIER, LAST = slice(0, BC - 1), slice(BC - 1, BC)

        @block.vector
        def _(dve):
            nc.vector.memset(wt1a[:, :], 0.0).then_inc(feat_cleared, 1)
            dve.wait_ge(ident_ready, 2)
            nc.vector.tensor_copy(ident_r[:, :], ident[:, :])
            nc.vector.tensor_copy(sel_r[:, :, :], fold[:, 0:F].unsqueeze(2).to_broadcast([P, F, H]))
            for s in range(SHIFTS):
                nc.vector.tensor_copy(rot_r[:, s, :], fold[:, s + 1:s + 1 + F])
            nc.vector.tensor_copy(rep_r[:, :, :],
                                  fold[:, 0:F].unsqueeze(1).to_broadcast([P, 4, F])).then_inc(consts_ready, 1)
            dve.wait_ge(w_loaded, 16 * W_LOADS)
            v = w0_sb.rearrange("p (i j) -> p i j", j=F)
            nc.vector.tensor_tensor(w0_sym.rearrange("p (i j) -> p i j", j=F), v,
                                    w0_sb.rearrange("p (i j) -> p j i", j=F), ALU.add).then_inc(w0_added, 1)
            nc.vector.tensor_copy(w1_mh.rearrange("p (m h) -> p m h", h=H),
                                  w1_sb.rearrange("p (h m) -> p m h", m=F))
            for r in range(4):
                nc.vector.tensor_scalar(w0_diag[:, r, :], w0_sb[:, 0:F * F:F + 1], 1.0, None, ALU.mult)
            dve.wait_ge(w0_added, 1)
            for s in range(1, SHIFTS + 1):
                scale = 0.5 if s == SHIFTS else 1.0
                split = F - s
                nc.vector.tensor_scalar(w0_pair[:, s - 1, 0:split], w0_sym[:, s:s + (F + 1) * (split - 1) + 1:F + 1],
                                        scale, None, ALU.mult)
                start = (F + 1) * split + s - F
                last = nc.vector.tensor_scalar(w0_pair[:, s - 1, split:F],
                                               w0_sym[:, start:start + (F + 1) * (s - 1) + 1:F + 1],
                                               scale, None, ALU.mult)
            last.then_inc(w0_folded, 1)

            for n in range(len(BATCHES)):
                dve.wait_ge(w_copied, 2 * (n + 1))
                if n == 0:
                    for q in (1, 3):
                        rows = slice(q * F, (q + 1) * F)
                        last = nc.vector.tensor_tensor(w0_sq_r[rows, :], w0_sq[rows, :], w0_sq_r[rows, :],
                                                       ALU.subtract)
                elif n == 1:
                    last = nc.vector.tensor_tensor(w0_lo[:, :, :], w0_t[:, :, :], w0_hi[:, :, :], ALU.subtract)
                else:
                    k = slice(4 * (n - 2), 4 * (n - 1))
                    last = nc.vector.tensor_tensor(w1_lo[:, k, :], w1_t[:, k, :], w1_hi[:, k, :], ALU.subtract)
                last.then_inc(w_split, 1)

            def squares_low(t):
                dve.wait_ge(squared, 2 * (t + 1))
                nc.vector.tensor_tensor(sq_r[H:P, :], p_x[H:P, :], sq_r[H:P, :], ALU.subtract).then_inc(sq_ready, 1)

            def multiply(t, p, first, s, other):
                g = pos(t, s)
                if spread(t, s, first):
                    rows = x_spread[SPREAD.index(s)]
                    dve.wait_ge(x_spread_loaded[SPREAD.index(s)], 16 * SPREAD_DMAS * (t - SPREAD_FROM + 1))
                else:
                    rows = pair[at(t, p, s, 2)]
                    dve.wait_ge(selected, g + 1)
                if not isinstance(t, int) or g >= NZ:
                    dve.wait_ge(contracted, g + 1 - NZ)
                nc.vector.tensor_tensor(z[:, at(t, p, s, NZ), :, :], rows[:, :, :],
                                        other.unsqueeze(1).to_broadcast([P, 2, C]),
                                        ALU.mult).then_inc(z_ready, 1)

            def low_part(entry, a):
                if entry is None or who(entry[0], entry[3], entry[2]) != "V":
                    return
                t, p, first, s = entry
                dve.wait_ge(zh_ready, count("VG", t, s, first))
                buf = at(t, p, s, NZ)
                nc.vector.tensor_tensor(z_lo[:, buf, a, :], z[:, buf, a, :], z_hi[:, buf, a, :],
                                        ALU.subtract).then_inc(zl_vector, 1)

            def add_up(t, before, acc, src, used):
                for half in range(2):
                    if half or not isinstance(t, int) or before > 0:
                        dve.wait_ge(used, before + half)
                    dst = acc[:, bass.ds(t // GPB, 1), :]
                    nc.vector.tensor_tensor(dst, dst, src[:, half * (C // 2):(half + 1) * (C // 2)].unsqueeze(1),
                                            ALU.add).then_inc(used, 1)

            def add_direct(t):
                dve.wait_ge(direct_ready, t + 1)
                add_up(t, t - 1, acc0, direct, direct_used)

            def add_rel1(t, p):
                dve.wait_ge(rel1_ready, t + 1)
                add_up(t, 2 * t, acc1, rel1[:, p, :], rel1_used)

            def dim_sums(dst, acc, groups):
                return nc.vector.tensor_reduce(dst[:, groups.start * P:groups.stop * P].rearrange("p (c b) -> p c b", b=P),
                                               acc[:, groups, :].rearrange("p c (d b) -> p c b d", b=P),
                                               AX.X, ALU.add)

            def even_sums(groups, chunks):
                dve.wait_ge(feat_cleared, 2)
                dve.wait_ge(direct_used, chunks)
                dim_sums(feat_a[H:P, :], acc0[H:P, :, :], groups)

            def odd_sums(groups):
                dim_sums(odd_feat[H:P, :], acc0[0:H, :, :], groups).then_inc(odd_summed, 1)

            def both_sums(groups, n):
                dve.wait_ge(odd_summed, n)
                cols = slice(groups.start * P, groups.stop * P)
                nc.vector.tensor_tensor(feat_a[H:P, cols], feat_a[H:P, cols], odd_feat[H:P, cols],
                                        ALU.add).then_inc(feat_ready, 1)

            def rel1_sums(groups, chunks):
                dve.wait_ge(rel1_used, 2 * chunks)
                dim_sums(feat_b, acc1, groups).then_inc(feat_ready, 1)

            dve.wait_ge(w_turned, len(BATCHES))
            nc.vector.memset(acc0[:, :, :], 0.0).then_inc(acc_cleared, 1)
            nc.vector.memset(acc1[:, :, :], 0.0).then_inc(acc_cleared, 1)
            dve.wait_ge(acc_cleared, 2)

            def step(t, p=None, first=None):
                p = t % 2 if p is None else p
                slots = slots_of(t)
                for s in range(NS):
                    if s in slots:
                        kind, k = SLOTS[s]
                        if (kind, k) == ("L1", 0):
                            dve.wait_ge(hid_ready, 2 * (t + 1))
                        if (kind, k) == ("L0", 0):
                            dve.wait_ge(x4_ready, t + 2)
                        multiply(t, p, first, s, x4[:, :] if kind == "L0" else hid2[:, p, :])
                        for a in (1, 0):
                            low_part(lagged(t, p, first, slots.index(s), LOW_LAG + a), a)
                    if s == S_SQUARE + 3 and has(t, 1):
                        squares_low(t + 1)
                    if s == S_STAGE + 2 and has(t, 2) and (t < PLAIN if isinstance(t, int) else first):
                        stage_low(dve, t + 2)
                    if isinstance(t, int) and (t, s) == (T - 2, 1):
                        even_sums(EARLIER, T - GPB)
                    if isinstance(t, int) and (t, s) == (T - 2, 5):
                        odd_sums(EARLIER)
                    if isinstance(t, int) and (t, s) == (T - 2, 9):
                        both_sums(EARLIER, 1)
                    if isinstance(t, int) and (t, s) == (T - 1, 5):
                        rel1_sums(EARLIER, T - GPB)
                    if s == 8 and p == 1 and has(t, 0):
                        add_direct(t)
                    if s == 6 and has(t, -1):
                        add_rel1(t - 1, 1 - p)
                if isinstance(t, int):
                    left = rest(t, LOW_LAG + 1)
                    for i, entry in enumerate(left):
                        for a in range(2):
                            if a == 1 or len(left) <= LOW_LAG or i > 0:
                                low_part(entry, a)

            steps(dve, step)
            even_sums(LAST, T)
            odd_sums(LAST)
            both_sums(LAST, 2)
            add_rel1(T - 1, (T - 1) % 2)
            rel1_sums(LAST, T)

        @block.tensor
        def _(pe):
            pe.wait_ge(ident_ready, 1)
            pe.wait_ge(w0_folded, 1)
            for n, batch in enumerate(BATCHES):
                if n >= 2:
                    pe.wait_ge(w_copied, 2 * (n - 1))
                for a in range(batch):
                    if n == 0:
                        src = w0_diag.rearrange("p r i -> p (r i)")
                    elif n == 1:
                        src = w0_pair[:, 4 * a:4 * a + 4, :].rearrange("p s i -> p (s i)")
                    else:
                        j = 4 * (n - 2) + a
                        src = w1_mh[:, j * P:(j + 1) * P]
                    last = nc.tensor.transpose(turned(n)[:, a * O:(a + 1) * O], src, ident[:, :])
                last.then_inc(w_turned, 1)
            pe.wait_ge(w_copied, 2 * len(BATCHES))
            pe.wait_ge(w_split, len(BATCHES))
            pe.wait_ge(consts_ready, 1)

            def transpose_chunk(t):
                pe.wait_ge(staged, t + 1)
                if not isinstance(t, int) or t > 0:
                    pe.wait_ge(sq_ready, t)
                for d in range(DPC):
                    last = nc.tensor.matmul(p_x[:, d * P:(d + 1) * P],
                                            stage[:, d, :, :, :].rearrange("p c l f -> p (c l f)"), ident_r[:, :],
                                            start=True, stop=True)
                last.then_inc(transposed, 1)

            def quadruple(t):
                pe.wait_ge(xhl0_ready, t + 1)
                nc.tensor.matmul(p_x[:, :], rep_r[0:2 * F, :, :].rearrange("p r i -> p (r i)"), xhl0[0:2 * F, :],
                                 start=True, stop=True).then_inc(quad_ready, 1)

            def select(t, p, first, s):
                kind, k = SLOTS[s]
                g = pos(t, s)
                x = xhl1[:, p, :] if kind == "L1" else xhl0[:, :]
                if spread(t, s, first):
                    return
                if (kind, k) == ("L1", len(SPREAD) if spread(t, 0, first) else 0):
                    pe.wait_ge(xhl1_ready, t + 1)
                if not isinstance(t, int) or g >= 2:
                    pe.wait_ge(z_ready, g - 1)
                for a in range(2):
                    rows = slice(a * 2 * F, (a + 1) * 2 * F)
                    j = 2 * k + a
                    pick = (sel_r[rows, 2 * j:2 * j + 2, :] if kind == "L1" else rot_r[rows, 4 * j:4 * j + 4, :]
                            ).rearrange("p a b -> p (a b)")
                    last = nc.tensor.matmul(pair[at(t, p, s, 2)][:, a, :], pick, x[rows, :],
                                            start=True, stop=True)
                steps_up = 1
                for before in reversed(slots_of(t)[:slots_of(t).index(s)]):
                    if not spread(t, before, first):
                        break
                    steps_up += 1
                last.then_inc(selected, steps_up)

            def squares(t):
                pe.wait_ge(sq_ready, t + 1)
                nc.tensor.matmul(p_out0[:, :], w0_sq_r[:, :], sq_r[:, :], start=False,
                                 stop=True).then_inc(out0_ready, 1)

            def contract(entry):
                if entry is None:
                    return
                t, p, first, s = entry
                kind, k = SLOTS[s]
                if (kind, k) == ("L0", 0) and (not isinstance(t, int) or t >= 0):
                    pe.wait_ge(direct_ready, t + 1)
                if (kind, k) == ("L1", 0) and (not isinstance(t, int) or t > 1):
                    pe.wait_ge(rel1_ready, t - 1)
                maker = who(t, s, first)
                if maker == "N":
                    pe.wait_ge(z_ready, pos(t, s) + 1)
                else:
                    pe.wait_ge(zh_ready, count("VG", t, s, first))
                buf = at(t, p, s, NZ)
                full, high, low = (w1_t, w1_hi, w1_lo) if kind == "L1" else (w0_t, w0_hi, w0_lo)
                dst = p_out1[:, p, :] if kind == "L1" else p_out0[:, :]
                tiles = F // 2 if kind == "L1" else SHIFTS // 4
                work = []
                for a in range(2):
                    j = 2 * k + a
                    if maker == "N":
                        work.append((full[:, j, :], z[:, buf, a, :], a, False))
                    else:
                        work += [(w[:, j, :], z_hi[:, buf, a, :], a, False) for w in (high, low)]
                if maker != "N":
                    work += [(high[:, 2 * k + a, :], z_lo[:, buf, a, :], a, True) for a in range(2)]
                for i, (w, x, a, x_low) in enumerate(work):
                    if maker == "V" and x_low:
                        pe.wait_ge(zl_vector, 2 * count("V", t, s, first) - 1 + a)
                    if maker == "G" and x_low and a == 0:
                        pe.wait_ge(zl_pool, count("G", t, s, first))
                    last = nc.tensor.matmul(dst, w, x, start=(k == 0 and i == 0),
                                            stop=(kind == "L1" and 2 * k + 2 == tiles and i == len(work) - 1))
                last.then_inc(contracted, 1)
                if (kind, k) == ("L0", 1):
                    squares(t + 1)

            def step(t, p=None, first=None):
                p = t % 2 if p is None else p
                slots = slots_of(t)
                for s in range(NS):
                    if s in slots:
                        select(t, p, first, s)
                        contract(lagged(t, p, first, slots.index(s), LAG))
                    if s == S_TURN and has(t, 2):
                        transpose_chunk(t + 2)
                    if s == S_QUAD and has(t, 2):
                        quadruple(t + 2)
                for entry in rest(t, LAG) if isinstance(t, int) else []:
                    contract(entry)

            steps(pe, step)

            pe.wait_ge(top_loaded, 16 * TOP_LOADS)
            pe.wait_ge(late_ident_ready, 1)
            pe.wait_ge(direct_ready, T)
            pe.wait_ge(sq_ready, T)
            for c in range(BC):
                bank = p_out0 if c < 4 else p_x
                last = nc.tensor.transpose(bank[0:DENSE, (c % 4) * P:(c % 4 + 1) * P], dense_sb[:, c, :], late_ident)
                if c % 4 == 3:
                    last.then_inc(dense_turned, 1)
            done = 0
            for half in range(2):
                pe.wait_ge(feat_ready, 2 + 2 * half)
                pe.wait_ge(dense_ready, half + 1)
                cols = slice(half * C, (half + 1) * C)
                for k in range(H1 // P):
                    if done >= 4:
                        pe.wait_ge(top_act, done - 3)
                    nc.tensor.matmul(top_bank(done), wt1a[:, k * P:(k + 1) * P], feat_a[:, cols], start=True, stop=False)
                    nc.tensor.matmul(top_bank(done), wt1b[:, k * P:(k + 1) * P], feat_b[:, cols], start=False,
                                     stop=True).then_inc(top_mm, 1)
                    done += 1
            for half in range(2):
                cols = slice(half * C, (half + 1) * C)
                for k in range(H2 // P):
                    pe.wait_ge(top_act, max(done - 3, 4 * (half + 1)))
                    for q in range(H1 // P):
                        last = nc.tensor.matmul(top_bank(done), wt2_sb[:, q, k * P:(k + 1) * P], h1_sb[:, q, cols],
                                                start=(q == 0), stop=(q == H1 // P - 1))
                    last.then_inc(top_mm, 1)
                    done += 1
            for half in range(2):
                cols = slice(half * C, (half + 1) * C)
                pe.wait_ge(top_act, max(done - 3, 8 + 2 * (half + 1)))
                for q in range(H2 // P):
                    last = nc.tensor.matmul(top_bank(done)[0:1, :], wt3_sb[:, q:q + 1], h2_sb[:, q, cols],
                                            start=(q == 0), stop=(q == H2 // P - 1))
                last.then_inc(top_mm, 1)
                done += 1


_FIRST = ["dense_ctx", "ids"]
_TABLES = [f"tbl_{i}" for i in range(F)]
_REST = ["L0_rec_W0", "L0_rec_b0", "L0_rec_W1", "L0_rec_b1", "W_top1", "b_top1", "W_top2", "b_top2", "W_top3"]


def kernel(**inputs):
    import numpy as np
    import concourse.bacc as bacc
    from concourse.bass_utils import run_bass_kernel_spmd

    nc = bacc.Bacc("TRN2", target_bir_lowering=False, num_devices=1)
    arrays, aps = {}, {}
    for name in _FIRST + _TABLES + _REST:
        a = np.ascontiguousarray(inputs[name])
        arrays[f"in_{name}"] = a
        aps[name] = nc.dram_tensor(f"in_{name}", a.shape, mybir.dt.from_np(a.dtype), kind="ExternalInput").ap()
    x_rows = nc.dram_tensor("x_rows", (ROWS_SPREAD, C), F32, kind="Internal").ap()
    out = nc.dram_tensor("out_y", (B, 1), F32, kind="ExternalOutput").ap()
    cin_tower(nc, aps["dense_ctx"], aps["ids"], [aps[n] for n in _TABLES], *[aps[n] for n in _REST], x_rows, out)
    return run_bass_kernel_spmd(nc, [arrays], core_ids=[0]).results[0]["out_y"]
```
